# Optimizing a Trainium2 kernel written in Bass

```python
import numpy as np
import jax
import jax.numpy as jnp

def _softmax(x, axis=-1):
    return jax.nn.softmax(x, axis=axis)

def _gelu(x):
    return jax.nn.gelu(x, approximate=True)

def _silu(x):
    return jax.nn.silu(x)

def _sigmoid(x):
    return jax.nn.sigmoid(x)

def _layernorm(x, axis=-1, eps=1e-05):
    m = jnp.mean(x, axis=axis, keepdims=True)
    v = jnp.var(x, axis=axis, keepdims=True)
    return (x - m) / jnp.sqrt(v + eps)

def _scatter_add(tgt, idx, src, axis=0):
    return tgt.at[idx].add(src)

def _segment_sum(src, seg, n):
    return jax.ops.segment_sum(src, seg, n)
kernel_name = 'mk_xattn_ffn_d2_seqx_r4_84fd2f'

def setup_inputs(seed: int=0):
    np.random.seed(seed)
    _w = jnp.asarray

    def _rec_inputs():
        import jax
        import jax.numpy as jnp
        _rk = jax.random.key(seed)
        x = -0.0002928 + 1 * jax.random.normal(jax.random.fold_in(_rk, 1), (8, 256, 256), jnp.float32)
        _lenS = 256 - jax.random.randint(jax.random.fold_in(_rk, 7), (8,), 0, max(1, 256 // 4) + 1, jnp.int32)
        _lenS2 = 256 - jax.random.randint(jax.random.fold_in(_rk, 8), (8,), 0, max(1, 256 // 4) + 1, jnp.int32)
        _ctx_1024P = jax.random.normal(jax.random.fold_in(_rk, 11), (8, 16, 256), jnp.float32)
        _ctx_1024c = jax.random.dirichlet(jax.random.fold_in(_rk, 511), 0.3 * jnp.ones((16,), jnp.float32), (8, 256))
        _ctx_1024t = jnp.einsum('bsk,bkd->bsd', _ctx_1024c, _ctx_1024P)
        _ctx_1024t = _ctx_1024t * jax.lax.rsqrt(jnp.mean(jnp.square(_ctx_1024t)) + 1e-12) * 0.953939
        ctx_1024 = -1.39393e-06 + 0.999914 * (_ctx_1024t + 0.3 * jax.random.normal(jax.random.fold_in(_rk, 611), (8, 256, 256), jnp.float32))
        return (x, ctx_1024)
    x, ctx_1024 = _rec_inputs()

    def _L0_xattn_setup():
        import jax, jax.numpy as jnp
        import numpy as np
        B, S, DIM, NH = (2, 512, 256, 8)
        DH = DIM // NH
        GATE_SOFT_CAP = 15.0
        BACKEND_EPS = 5e-05
        NORM_EPS = 1e-06

        def _mlstm_parallel(q, k, v, i_pre, f_pre):
            log_fg = jax.nn.log_sigmoid(f_pre)
            lf_cs = jnp.cumsum(log_fg, axis=-1)
            lf = jnp.concatenate([jnp.zeros_like(lf_cs[..., :1]), lf_cs], axis=-1)
            log_d = lf[..., 1:, None] - lf[..., None, 1:] + i_pre[..., None, :]
            t_idx = jnp.arange(q.shape[2])
            mask = t_idx[:, None] >= t_idx[None, :]
            log_d = jnp.where(mask, log_d, -jnp.inf)
            m = jnp.max(log_d, axis=-1, keepdims=True)
            d_mat = jnp.exp(log_d - m)
            scores = jnp.einsum('bhtd,bhsd->bhts', q, k) * (1.0 / np.sqrt(DH))
            s_mat = scores * d_mat
            denom = jnp.maximum(jnp.abs(jnp.sum(s_mat, axis=-1, keepdims=True)), jnp.exp(-m)) + BACKEND_EPS
            return jnp.einsum('bhts,bhsd->bhtd', s_mat, v) / denom
        key = jax.random.key(seed)
        kq, kk, kv, kw = jax.random.split(key, 4)
        q = jax.random.normal(kq, (B, S, DIM), dtype=jnp.float32)
        k = jax.random.normal(kk, (B, S, DIM), dtype=jnp.float32)
        v = jax.random.normal(kv, (B, S, DIM), dtype=jnp.float32)
        ifgate_w = 0.02 * jax.random.normal(kw, (2 * NH, 3 * DIM), dtype=jnp.float32)
        ifgate_b = jnp.concatenate([jnp.full((NH,), -10.0, dtype=jnp.float32), jnp.linspace(3.0, 6.0, NH, dtype=jnp.float32)])
        outnorm_w = jnp.zeros((DIM,), dtype=jnp.float32)
        return {'q': q, 'k': k, 'v': v, 'ifgate_w': ifgate_w, 'ifgate_b': ifgate_b, 'outnorm_w': outnorm_w}
    _L0_xattn_all = _L0_xattn_setup()
    _L0_xattn_in = {k: v for k, v in _L0_xattn_all.items() if k in ('ifgate_w', 'ifgate_b', 'outnorm_w')}
    del _L0_xattn_all

    def _L0_ffn_setup():
        import jax, jax.numpy as jnp
        import numpy as np
        EPS = 1e-05

        def rmsnorm(x):
            return x * jax.lax.rsqrt(jnp.mean(x * x, axis=-1, keepdims=True) + EPS)

        def act_quant(x):
            scale = 127.0 / jnp.clip(jnp.max(jnp.abs(x), axis=-1, keepdims=True), 1e-05)
            q = jnp.clip(jnp.round(x * scale), -128.0, 127.0) / scale
            return x + jax.lax.stop_gradient(q - x)

        def weight_quant(w):
            scale = 1.0 / jnp.clip(jnp.mean(jnp.abs(w)), 1e-05)
            q = jnp.clip(jnp.round(w * scale), -1.0, 1.0) / scale
            return w + jax.lax.stop_gradient(q - w)

        def bitlinear(x, w, b):
            xq = act_quant(rmsnorm(x))
            wq = weight_quant(w)
            return jnp.einsum('bsd,fd->bsf', xq, wq) + b
        key = jax.random.key(seed)
        k0, k1, k2 = jax.random.split(key, 3)
        B, S, D, F = (2, 2048, 256, 1024)
        x = jax.random.normal(k0, (B, S, D), dtype=jnp.float32)
        w1 = jax.random.normal(k1, (F, D), dtype=jnp.float32) * (1.0 / np.sqrt(D))
        b1 = jnp.zeros((F,), dtype=jnp.float32)
        w2 = jax.random.normal(k2, (D, F), dtype=jnp.float32) * (1.0 / np.sqrt(F))
        b2 = jnp.zeros((D,), dtype=jnp.float32)
        return {'x': x, 'w1': w1, 'b1': b1, 'w2': w2, 'b2': b2}
    _L0_ffn_all = _L0_ffn_setup()
    _L0_ffn_in = {k: v for k, v in _L0_ffn_all.items() if k in ('w1', 'b1', 'w2', 'b2')}
    del _L0_ffn_all

    def _L1_xattn_setup():
        import jax, jax.numpy as jnp
        import numpy as np
        EPS = 1e-08
        FORGET = 1.0 - 10 * EPS

        def _phi(x):
            return (jax.nn.elu(x) + 1.0) ** 5
        key = jax.random.key(seed)
        k1, k2, k3 = jax.random.split(key, 3)
        B, T, C = (8, 512, 256)
        return {'query': jax.random.normal(k1, (B, T, C), dtype=jnp.float32), 'key': jax.random.normal(k2, (B, T, C), dtype=jnp.float32), 'value': jax.random.normal(k3, (B, T, C), dtype=jnp.float32)}
    _L1_xattn_all = _L1_xattn_setup()
    _L1_xattn_in = {k: v for k, v in _L1_xattn_all.items() if k in ()}
    del _L1_xattn_all

    def _L1_ffn_setup():
        import jax, jax.numpy as jnp
        import numpy as np
        D_MODEL = 256
        D_FF = 1024
        NUM_EXPERTS = 8
        TOP_K = 2
        key = jax.random.key(seed)
        ks = jax.random.split(key, 8)
        s_in = 1.0 / np.sqrt(D_MODEL)
        s_ff = 1.0 / np.sqrt(D_FF)
        x = jax.random.normal(ks[0], (2, 512, D_MODEL), dtype=jnp.float32)
        Wg = jax.random.uniform(ks[1], (D_MODEL, NUM_EXPERTS), minval=-s_in, maxval=s_in, dtype=jnp.float32)
        bg = jax.random.uniform(ks[2], (NUM_EXPERTS,), minval=-s_in, maxval=s_in, dtype=jnp.float32)
        W1 = jax.random.uniform(ks[3], (NUM_EXPERTS, D_MODEL, D_FF), minval=-s_in, maxval=s_in, dtype=jnp.float32)
        b1 = jax.random.uniform(ks[4], (NUM_EXPERTS, D_FF), minval=-s_in, maxval=s_in, dtype=jnp.float32)
        W2 = jax.random.uniform(ks[5], (NUM_EXPERTS, D_FF, D_MODEL), minval=-s_ff, maxval=s_ff, dtype=jnp.float32)
        b2 = jax.random.uniform(ks[6], (NUM_EXPERTS, D_MODEL), minval=-s_ff, maxval=s_ff, dtype=jnp.float32)
        return {'x': x, 'Wg': Wg, 'bg': bg, 'W1': W1, 'b1': b1, 'W2': W2, 'b2': b2}
    _L1_ffn_all = _L1_ffn_setup()
    _L1_ffn_in = {k: v for k, v in _L1_ffn_all.items() if k in ('Wg', 'bg', 'W1', 'b1', 'W2', 'b2')}
    del _L1_ffn_all
    return {'x': x, 'ctx_1024': ctx_1024, 'L0_xattn_ifgate_w': _L0_xattn_in['ifgate_w'], 'L0_xattn_ifgate_b': _L0_xattn_in['ifgate_b'], 'L0_xattn_outnorm_w': _L0_xattn_in['outnorm_w'], 'L0_ffn_w1': _L0_ffn_in['w1'], 'L0_ffn_b1': _L0_ffn_in['b1'], 'L0_ffn_w2': _L0_ffn_in['w2'], 'L0_ffn_b2': _L0_ffn_in['b2'], 'L1_ffn_Wg': _L1_ffn_in['Wg'], 'L1_ffn_bg': _L1_ffn_in['bg'], 'L1_ffn_W1': _L1_ffn_in['W1'], 'L1_ffn_b1': _L1_ffn_in['b1'], 'L1_ffn_W2': _L1_ffn_in['W2'], 'L1_ffn_b2': _L1_ffn_in['b2']}

def reference(x, ctx_1024, L0_xattn_ifgate_w, L0_xattn_ifgate_b, L0_xattn_outnorm_w, L0_ffn_w1, L0_ffn_b1, L0_ffn_w2, L0_ffn_b2, L1_ffn_Wg, L1_ffn_bg, L1_ffn_W1, L1_ffn_b1, L1_ffn_W2, L1_ffn_b2):
    import jax
    import jax.numpy as jnp

    def _L0_xattn_ref(q, k, v, ifgate_w, ifgate_b, outnorm_w):
        import jax, jax.numpy as jnp
        import numpy as np
        B, S, DIM, NH = (2, 512, 256, 8)
        DH = DIM // NH
        GATE_SOFT_CAP = 15.0
        BACKEND_EPS = 5e-05
        NORM_EPS = 1e-06

        def _mlstm_parallel(q, k, v, i_pre, f_pre):
            log_fg = jax.nn.log_sigmoid(f_pre)
            lf_cs = jnp.cumsum(log_fg, axis=-1)
            lf = jnp.concatenate([jnp.zeros_like(lf_cs[..., :1]), lf_cs], axis=-1)
            log_d = lf[..., 1:, None] - lf[..., None, 1:] + i_pre[..., None, :]
            t_idx = jnp.arange(q.shape[2])
            mask = t_idx[:, None] >= t_idx[None, :]
            log_d = jnp.where(mask, log_d, -jnp.inf)
            m = jnp.max(log_d, axis=-1, keepdims=True)
            d_mat = jnp.exp(log_d - m)
            scores = jnp.einsum('bhtd,bhsd->bhts', q, k) * (1.0 / np.sqrt(DH))
            s_mat = scores * d_mat
            denom = jnp.maximum(jnp.abs(jnp.sum(s_mat, axis=-1, keepdims=True)), jnp.exp(-m)) + BACKEND_EPS
            return jnp.einsum('bhts,bhsd->bhtd', s_mat, v) / denom
        b, s, dim = q.shape
        gate_in = jnp.concatenate([q, k, v], axis=-1)
        pre = gate_in @ ifgate_w.T + ifgate_b
        pre = GATE_SOFT_CAP * jnp.tanh(pre / GATE_SOFT_CAP)
        i_pre = pre[..., :NH].transpose(0, 2, 1)
        f_pre = pre[..., NH:].transpose(0, 2, 1)
        qh = q.reshape(b, s, NH, DH).transpose(0, 2, 1, 3)
        kh = k.reshape(b, s, NH, DH).transpose(0, 2, 1, 3)
        vh = v.reshape(b, s, NH, DH).transpose(0, 2, 1, 3)
        h = _mlstm_parallel(qh, kh, vh, i_pre, f_pre)
        rrms = jax.lax.rsqrt(jnp.mean(h * h, axis=-1, keepdims=True) + NORM_EPS)
        gain = (1.0 + outnorm_w).reshape(1, NH, 1, DH)
        h = h * rrms * gain
        return h.transpose(0, 2, 1, 3).reshape(b, s, dim)

    def _L0_ffn_ref(x, w1, b1, w2, b2):
        import jax, jax.numpy as jnp
        import numpy as np
        EPS = 1e-05

        def rmsnorm(x):
            return x * jax.lax.rsqrt(jnp.mean(x * x, axis=-1, keepdims=True) + EPS)

        def act_quant(x):
            scale = 127.0 / jnp.clip(jnp.max(jnp.abs(x), axis=-1, keepdims=True), 1e-05)
            q = jnp.clip(jnp.round(x * scale), -128.0, 127.0) / scale
            return x + jax.lax.stop_gradient(q - x)

        def weight_quant(w):
            scale = 1.0 / jnp.clip(jnp.mean(jnp.abs(w)), 1e-05)
            q = jnp.clip(jnp.round(w * scale), -1.0, 1.0) / scale
            return w + jax.lax.stop_gradient(q - w)

        def bitlinear(x, w, b):
            xq = act_quant(rmsnorm(x))
            wq = weight_quant(w)
            return jnp.einsum('bsd,fd->bsf', xq, wq) + b
        h = bitlinear(x, w1, b1)
        h = jax.nn.gelu(h, approximate=False)
        return bitlinear(h, w2, b2)

    def _L1_xattn_ref(query, key, value):
        import jax, jax.numpy as jnp
        import numpy as np
        EPS = 1e-08
        FORGET = 1.0 - 10 * EPS

        def _phi(x):
            return (jax.nn.elu(x) + 1.0) ** 5
        B, T, C = query.shape
        q = _phi(query)
        k = _phi(key)
        t_idx = jnp.arange(T)
        dt = (t_idx[:, None] - t_idx[None, :]).astype(jnp.float32)
        logf = jnp.log(jnp.float32(FORGET))
        decay = jnp.where(dt >= 0, jnp.exp(dt * logf), 0.0)
        scores = jnp.einsum('btc,bsc->bts', q, k) * decay
        scale = scores.sum(axis=-1) + EPS
        out = jnp.einsum('bts,bsc->btc', scores, value) / scale[..., None]
        return out

    def _L1_ffn_ref(x, Wg, bg, W1, b1, W2, b2):
        import jax, jax.numpy as jnp
        import numpy as np
        D_MODEL = 256
        D_FF = 1024
        NUM_EXPERTS = 8
        TOP_K = 2
        gate_logits = jnp.einsum('bsd,de->bse', x, Wg) + bg
        gate_probs = jax.nn.softmax(gate_logits, axis=-1)
        topk_probs, topk_idx = jax.lax.top_k(gate_probs, TOP_K)
        topk_probs = topk_probs / jnp.sum(topk_probs, axis=-1, keepdims=True)
        onehot = jax.nn.one_hot(topk_idx, NUM_EXPERTS, dtype=x.dtype)
        weights = jnp.einsum('bske,bsk->bse', onehot, topk_probs)
        h = jnp.einsum('bsd,edf->bsef', x, W1) + b1
        h = jax.nn.gelu(h, approximate=False)
        y = jnp.einsum('bsef,efd->bsed', h, W2) + b2
        return jnp.einsum('bsed,bse->bsd', y, weights)
    x = x + _L0_xattn_ref(_layernorm(x, axis=-1), ctx_1024, ctx_1024, L0_xattn_ifgate_w, L0_xattn_ifgate_b, L0_xattn_outnorm_w)
    x = x + _L0_ffn_ref(_layernorm(x, axis=-1), L0_ffn_w1, L0_ffn_b1, L0_ffn_w2, L0_ffn_b2)
    x = x + _L1_xattn_ref(_layernorm(x, axis=-1), ctx_1024, ctx_1024)
    x = x + _L1_ffn_ref(_layernorm(x, axis=-1), L1_ffn_Wg, L1_ffn_bg, L1_ffn_W1, L1_ffn_b1, L1_ffn_W2, L1_ffn_b2)
    return x

_drawn_inputs = setup_inputs


def setup_inputs(seed=0):
    import zlib

    import numpy as np

    out = dict(_drawn_inputs(seed))
    spreads = {'L0_xattn_outnorm_w': (0.0, 0.1), 'L0_ffn_b1': (0.0, 0.1), 'L0_ffn_b2': (0.0, 0.1)}
    factors = {'L1_ffn_bg': 3.573, 'L1_ffn_b1': 8.0, 'L1_ffn_b2': 7.926}
    for name, (base, spread) in spreads.items():
        noise = np.random.default_rng([zlib.crc32(name.encode()), seed]).standard_normal(out[name].shape)
        drawn = base * np.exp(spread * noise) if base else spread * noise
        out[name] = jnp.asarray(drawn.astype(out[name].dtype))
    for name, factor in factors.items():
        out[name] = (out[name] * factor).astype(out[name].dtype)
    return out
```

```python
import math
import numpy as np
import concourse.bass as bass
from concourse import mybir
from contextlib import ExitStack

F32, BF16, I32 = mybir.dt.float32, mybir.dt.bfloat16, mybir.dt.int32
ALU = mybir.AluOpType
ACT = mybir.ActivationFunctionType
AX = mybir.AxisListType

P = 128
B, S, D = 8, 256, 256
T = B * S
NT = T // P
TB = S // P
NC = D // P
NH, DH = 8, 32
NBH = B * NH
VH = DH + 1
VA = NH * VH
F0 = 1024
NF0 = F0 // P
E, FE = 8, 1024
NF = FE // P
BLK = 256
BT = BLK // P
NBLK = (2 * T + E * (BLK - 1)) // BLK
LN_EPS = 1e-5
LOG_FORGET = float(np.log(np.float32(1.0 - 1e-7)))
MAGIC = 1.5 * 2.0 ** 23
CAP = 15.0
LOWEST = -3.0e38
GT = 512
NG = T // GT
SW = S + P
SPLIT_PIECES = 4


class Chain:

    def __init__(self, eng, sem):
        self.eng, self.sem, self.base, self.n, self.entry = eng, sem, 0, 0, 0

    def __call__(self, ins):
        self.n += 1
        ins.then_inc(self.sem, 1)
        self.eng.wait_ge(self.sem, self.base + self.n)

    def enter(self):
        self.entry = self.base + self.n

    def loop(self, it, steps):
        self.base, self.n = self.entry + it * steps, 0

    def passed(self, steps):
        assert self.n == steps, (self.n, steps)

    def leave(self, its, steps):
        self.base, self.n = self.entry + its * steps, 0


class Space:

    def __init__(self, *pools):
        self.pools = [[p, 0, p.shape[1]] for p in pools]

    def cut(self, *shape, dt=F32, pool=None):
        n = int(np.prod(shape[1:]))
        words = (n + 1) // 2 if dt == BF16 else n
        for k, entry in enumerate(self.pools):
            view, at, size = entry
            if at + words <= size and pool in (None, k):
                entry[1] += words
                v = view[0:shape[0], at:at + words]
                break
        else:
            raise AssertionError(("no room", shape, [(a, s) for _, a, s in self.pools]))
        if dt != F32:
            v = v.bitcast(dt)
        if len(shape) > 2:
            names = "abcd"[:len(shape) - 1]
            v = v.rearrange(f"p ({' '.join(names)}) -> p {' '.join(names)}",
                            **{names[k]: shape[k + 1] for k in range(len(names) - 1)})
        return v


def row(view, i):
    v = view[:, bass.ds(i, 1)]
    if len(v.shape) == 3:
        return v.rearrange("p a n -> p (a n)")
    return v.rearrange("p a m n -> p (a m) n") if len(v.shape) == 4 else v


def tile_of(view, i):
    return view[:, i] if isinstance(i, int) else row(view, i)


def col_of(mv, i):
    return tile_of(mv, i)[:, 0:1]


def cell(v, i):
    return v[:, i:i + 1] if isinstance(i, int) else v[:, bass.ds(i, 1)]


def flat(v):
    return v.rearrange("p a n -> p (a n)") if len(v.shape) == 3 else v.rearrange("p a b n -> p (a b n)")


def wide(v, n):
    return v.unsqueeze(len(v.shape)).broadcast_to([*v.shape, n])


def program(nc, A, out):
    cx = ExitStack()
    with cx:
        def sb(name, shape, dt=F32):
            return cx.enter_context(nc.sbuf_tensor(name, shape, dt))

        x_all = sb("x_all", [P, NT, D])
        vaug_t = sb("vaug", [P, NT * VA])
        region_t = sb("region", [P, NT * D])
        w1hi = sb("w1hi", [P, E, NC * FE], BF16)
        w1lo = sb("w1lo", [P, E, NC * FE], BF16)
        w2pair = sb("w2pair", [P, 2 * E * NF * D], BF16)
        aux_t = sb("aux", [P, 4864])
        wstage = sb("wstage", [P, NC * FE])
        ident = sb("ident", [P, P])
        identb = sb("identb", [P, P], BF16)
        ones_f = sb("ones_f", [P, P])
        stats = sb("stats", [P, NT, 6])
        mv = sb("mv", [P, NT, 2])
        veps = sb("veps", [P, NT])
        rstd = sb("rstd", [P, NT])
        rr = sb("rr", [P, NT])
        mhalf = sb("mhalf", [P, NT * NH])
        vaug = vaug_t[:, :].rearrange("p (k n) -> p k n", k=NT)
        w2v = w2pair[:, :].rearrange("p (a e n) -> p a e n", a=2, e=E)
        w2hi, w2lo = w2v[:, 0], w2v[:, 1]
        scratch = w2pair[:, :].bitcast(F32)
        region, aux, vaug_flat = region_t[:, :], aux_t[:, :], vaug_t[:, :]
        row_buf = nc.dram_tensor("row_buf", [NBLK * BLK, 2 * D], BF16, kind="Internal").ap()
        y_buf = nc.dram_tensor("y_buf", [NBLK * BLK, D], F32, kind="Internal").ap()

        w_in = cx.enter_context(nc.semaphore("w_in"))
        w_split = cx.enter_context(nc.semaphore("w_split"))
        w_chain = cx.enter_context(nc.semaphore("w_chain"))
        zero_in = cx.enter_context(nc.semaphore("zero_in"))

        passed_gate = cx.enter_context(nc.semaphore("passed_gate"))

        def gate(pool):
            pool.sem_inc(passed_gate, 1)

        def layer_stats(dve, chain, var_ready):
            for i in range(NT):
                last = dve.bn_stats(stats[:, i, :], x_all[:, i, :])
            chain(last)
            for i in range(NT):
                last = dve.bn_aggr(mv[:, i, :], stats[:, i, :])
            chain(last)
            dve.tensor_scalar(veps[:, :], mv[:, :, 1], LN_EPS, None, ALU.add).then_inc(var_ready, 1)

        def split_piece(pool, n, k, hi, lo):
            if k == 0:
                pool.wait_ge(w_in, 16 * n + 16)
                gate(pool)
            w = slice(k * NC * FE // SPLIT_PIECES, (k + 1) * NC * FE // SPLIT_PIECES)
            pool.tensor_copy(hi[:, w], wstage[:, w]).then_inc(w_chain, 1)
            pool.wait_ge(w_chain, n * SPLIT_PIECES + k + 1)
            last = pool.tensor_tensor(lo[:, w], wstage[:, w], hi[:, w], ALU.subtract)
            if k == SPLIT_PIECES - 1:
                last.then_inc(w_split, 1)

        def load_w(sp, n):
            if not isinstance(n, int) or n:
                sp.wait_ge(w_split, n)
            sp.dma_start(wstage[:, :], A["wall"][bass.ds(n, 1)].rearrange("a p n -> p (a n)")).then_inc(w_in, 16)

        space = Space(scratch)
        bT = space.cut(P, TB, NBH)
        emT = space.cut(P, TB, NBH)
        parts = space.cut(P, S, dt=BF16)
        parts2 = space.cut(P, S, dt=BF16)
        pick = space.cut(P, NBH, dt=BF16)
        gain = space.cut(P, D)
        after_gates = space.pools[0][1]
        qT = region.rearrange("p (c t) -> p c t", c=NC)
        with ExitStack() as c:
            sem = lambda n: c.enter_context(nc.semaphore("g_" + n))
            x_in, ctx_in, small_in = sem("x_in"), sem("ctx_in"), sem("small_in")
            ct_in = [sem("ct_in0"), sem("ct_in1")]
            made, ch, chp = sem("made"), sem("dve_chain"), sem("pool_chain")
            var_ready, rstd_ready, const_ready = sem("var_ready"), sem("rstd_ready"), sem("const_ready")
            xn_ready, tp_ready, qt_ready, gates_done = sem("xn_ready"), sem("tp_ready"), sem("qt_ready"), sem("gates_done")
            pre_ready, pre_moved, th_ready, lg_ready = sem("pre_ready"), sem("pre_moved"), sem("th_ready"), sem("lg_ready")
            dm_ready, em_ready, gt_ready, b_ready = sem("dm_ready"), sem("em_ready"), sem("gt_ready"), sem("b_ready")
            tpp = c.enter_context(nc.psum_tensor("tpp", [P, 2, NC, GT], F32))
            gp = c.enter_context(nc.psum_tensor("gp", [P, 2, GT], F32))
            xn = space.cut(P, 2, GT // P, D)
            ctg = space.cut(P, 2, NC, GT)
            wif = space.cut(P, 6, 2 * NH)
            ifb = space.cut(P, 1)
            presb = space.cut(2 * NH, T)
            pre, th, ex, soft, L, bb, M, dm, em, nM, r1, ones_s = (space.cut(P, S) for _ in range(12))
            mid = space.cut(P, S, dt=BF16)
            wkv = space.cut(P, 2, 2 * NH)
            zeros = space.cut(P, 512)
            h = slice(0, NBH)
            GTT = GT // P

            with nc.Block() as block:
                @block.sync
                def _(sp):
                    xv = A["x"].rearrange("(k p) d -> p k d", p=P)
                    for k in range(4):
                        sp.dma_start(x_all[:, 4 * k:4 * k + 4, :], xv[:, 4 * k:4 * k + 4, :]).then_inc(x_in, 16)
                    sp.dma_start(wif, A["ifwT"].rearrange("(c p) n -> p c n", p=P)).then_inc(small_in, 16)
                    sp.dma_start(ifb, A["ifb"]).then_inc(small_in, 16)
                    sp.dma_start(gain, A["outnorm"].partition_broadcast(P)).then_inc(small_in, 16)
                    ctv = A["ctxT"].rearrange("(c p) t -> p c t", p=P)
                    with sp.Fori(0, NG // 2) as k:
                        for u in range(2):
                            gi = 2 * k + u
                            sp.wait_ge(gates_done, gi + 1)
                            sp.dma_start(ctg[:, u], ctv[:, :, bass.ds(gi * GT, GT)]).then_inc(ct_in[u], 16)
                    load_w(sp, 0)
                    sp.wait_ge(pre_ready, NG + 2)
                    for gate in range(2):
                        for b in range(B):
                            r0 = gate * NBH + b * NH
                            sp.dma_start(pre[r0:r0 + NH, :], presb[gate * NH:(gate + 1) * NH, b * S:(b + 1) * S]).then_inc(pre_moved, 16)
                    for k in range(NT):
                        sp.dma_start(vaug[:, k, :].rearrange("p (h c) -> p h c", h=NH)[:, :, 0:DH],
                                     A["ctx"][k * P:(k + 1) * P, :].rearrange("p (h c) -> p h c", h=NH)).then_inc(ctx_in, 16)
                    sp.wait_ge(const_ready, 1)
                    with sp.Fori(0, NBLK) as k:
                        for t in range(BT):
                            sp.dma_start(row_buf[bass.ds(k * BLK + t * P, P), :], zeros.bitcast(BF16)[:, 0:2 * D]).then_inc(zero_in, 16)
                    sp.wait_ge(ctx_in, 16 * NT)

                @block.gpsimd
                def _(pool):
                    chain = Chain(pool, chp)
                    pool.memset(zeros, 0.0).then_inc(const_ready, 1)
                    pool.memset(ident[:, :], 0.0)
                    pool.memset(pick, 0.0)
                    pool.memset(mhalf[:, :], -0.5)
                    pool.memset(ones_f[:, :], 1.0)
                    chain(pool.memset(ones_s, 1.0))
                    chain(pool.affine_select(out=pick, in_=pick, compare_op=ALU.not_equal, fill=1.0, base=0,
                                             pattern=[[-1, NBH]], channel_multiplier=1))
                    chain(pool.affine_select(out=ident[:, :], in_=ident[:, :], compare_op=ALU.not_equal, fill=1.0, base=0,
                                             pattern=[[-1, P]], channel_multiplier=1))
                    chain(pool.affine_select(out=pick, in_=pick, compare_op=ALU.not_equal, fill=1.0, base=-NBH,
                                             pattern=[[-1, NBH]], channel_multiplier=1))
                    pool.tensor_copy(identb[:, :], ident[:, :]).then_inc(made, 1)
                    pool.memset(vaug_t[:, :].rearrange("p (n c) -> p n c", c=VH)[:, :, DH:VH], 1.0).then_inc(made, 1)
                    pool.memset(parts2, 0.0).then_inc(made, 1)
                    pool.wait_ge(var_ready, 1)
                    pool.tensor_tensor(rstd[:, :], veps[:, :], mhalf[:, 0:NT], ALU.pow).then_inc(rstd_ready, 1)

                @block.tensor
                def _(pe):
                    pe.sem_inc(gates_done, 2)
                    pe.wait_ge(made, 3)
                    pe.wait_ge(small_in, 48)
                    pe.wait_ge(ch, 5)
                    with pe.Fori(0, NG // 2) as k:
                        for u in range(2):
                            gi = 2 * k + u
                            pe.wait_ge(xn_ready, gi + 1)
                            pe.wait_ge(qt_ready, gi + 1)
                            for cc in range(NC):
                                for t in range(GTT):
                                    last = pe.transpose(tpp[:, u, cc, t * P:(t + 1) * P], xn[:, u, t, cc * P:(cc + 1) * P], ident[:, :])
                            last.then_inc(tp_ready, 1)
                            pe.wait_ge(ct_in[u], 16 * k + 16)
                            pe.wait_ge(pre_ready, gi + 1)
                            for cc in range(NC):
                                pe.matmul(gp[0:2 * NH, u, :], wkv[:, cc, :], ctg[:, u, cc, :], start=(cc == 0), stop=False)
                            pe.wait_ge(qt_ready, gi + 3)
                            for cc in range(NC):
                                last = pe.matmul(gp[0:2 * NH, u, :], wif[:, cc, :], qT[:, cc, bass.ds(gi * GT, GT)], start=False, stop=(cc == NC - 1))
                            last.then_inc(gates_done, 1)
                    pe.wait_ge(b_ready, 1)
                    pe.wait_ge(em_ready, 1)
                    for t in range(TB):
                        pe.transpose(tpp[:, 0, 0, t * NBH:(t + 1) * NBH], bb[h, t * P:(t + 1) * P], ident[h, h])
                        last = pe.transpose(tpp[:, 0, 0, (TB + t) * NBH:(TB + 1 + t) * NBH], em[h, t * P:(t + 1) * P], ident[h, h])
                    last.then_inc(gt_ready, 1)

                @block.vector
                def _(dve):
                    chain = Chain(dve, ch)
                    dve.wait_ge(x_in, 64)
                    layer_stats(dve, chain, var_ready)
                    dve.wait_ge(small_in, 48)
                    chain(dve.tensor_tensor(wkv, wif[:, 2:4, :], wif[:, 4:6, :], ALU.add))
                    chain(dve.tensor_scalar(ifb, ifb, 1.0 / CAP, None, ALU.mult))
                    chain(dve.tensor_scalar(gain, gain, 1.0, None, ALU.add))
                    dve.sem_inc(pre_ready, 2)
                    dve.wait_ge(rstd_ready, 1)
                    with dve.Fori(0, NG // 2) as k:
                        for u in range(2):
                            gi = 2 * k + u
                            dve.wait_ge(qt_ready, gi + 1)
                            for t in range(GTT):
                                i = gi * GTT + t
                                last = dve.tensor_scalar(xn[:, u, t, :], row(x_all, i), row(mv, i)[:, 0:1], rstd[:, bass.ds(i, 1)],
                                                         ALU.subtract, ALU.mult)
                            last.then_inc(xn_ready, 1)
                            dve.wait_ge(gates_done, gi + 3)
                            dve.tensor_copy(presb[:, bass.ds(gi * GT, GT)], gp[0:2 * NH, u, :]).then_inc(pre_ready, 1)
                    dve.wait_ge(lg_ready, 1)
                    dve.wait_ge(made, 3)
                    chain(dve.tensor_tensor_scan(L[h], ones_s[h], soft[h], 0.0, ALU.mult, ALU.add))
                    dve.scalar_tensor_tensor(bb[h], th[h], CAP, L[h], ALU.mult, ALU.add).then_inc(b_ready, 1)
                    dve.wait_ge(b_ready, 1)
                    chain(dve.tensor_tensor_scan(M[h], bb[h], bb[h], LOWEST, ALU.max, ALU.max))
                    dve.tensor_tensor(dm[h], L[h], M[h], ALU.subtract).then_inc(dm_ready, 1)
                    chain(dve.tensor_scalar(nM[h], M[h], -1.0, None, ALU.mult))
                    chain(dve.tensor_copy(parts[h], nM[h]))
                    chain(dve.tensor_tensor(r1[h], nM[h], parts[h], ALU.subtract))
                    chain(dve.tensor_copy(mid[h], r1[h]))
                    chain(dve.tensor_copy(parts[NBH:2 * NBH], mid[h]))
                    chain(dve.tensor_tensor(parts2[h], r1[h], mid[h], ALU.subtract))
                    dve.wait_ge(gt_ready, 1)
                    dve.tensor_copy(bT, tpp[:, 0, 0, 0:TB * NBH].rearrange("p (t n) -> p t n", t=TB))
                    chain(dve.tensor_copy(emT, tpp[:, 0, 0, TB * NBH:2 * TB * NBH].rearrange("p (t n) -> p t n", t=TB)))

                @block.scalar
                def _(act):
                    act.sem_inc(qt_ready, 2)
                    with act.Fori(0, NG // 2) as k:
                        for u in range(2):
                            gi = 2 * k + u
                            act.wait_ge(tp_ready, gi + 1)
                            act.activation(qT[:, 0, bass.ds(gi * GT, GT)], tpp[:, u, 0, :], ACT.Copy)
                            act.activation(qT[:, 1, bass.ds(gi * GT, GT)], tpp[:, u, 1, :], ACT.Copy).then_inc(qt_ready, 1)
                    act.wait_ge(pre_moved, 16 * 2 * B)
                    act.wait_ge(ch, 5)
                    act.activation(th, pre, ACT.Tanh, bias=ifb, scale=1.0 / CAP).then_inc(th_ready, 1)
                    act.wait_ge(th_ready, 1)
                    act.activation(ex[h], th[NBH:2 * NBH], ACT.Exp, scale=-CAP).then_inc(th_ready, 1)
                    act.wait_ge(th_ready, 2)
                    act.activation(soft[h], ex[h], ACT.Ln, bias=1.0).then_inc(lg_ready, 1)
                    act.wait_ge(dm_ready, 1)
                    act.activation(em[h], dm[h], ACT.Exp).then_inc(em_ready, 1)

        with ExitStack() as c:
            sem = lambda n: c.enter_context(nc.semaphore("m_" + n))
            qk_in = [sem("qk_in0"), sem("qk_in1")]
            decay_ready, s_ready, exp_done, masked = sem("decay_ready"), sem("s_ready"), sem("exp_done"), sem("masked")
            mul_done, pv_done, pv_read, sq_done = sem("mul_done"), sem("pv_done"), sem("pv_read"), sem("sq_done")
            ch, t_ready, r_ready, y_ready, gained = sem("dve_chain"), sem("t_ready"), sem("r_ready"), sem("y_ready"), sem("gained")
            wp = c.enter_context(nc.psum_tensor("wp", [P, 2, 2, S], F32))
            spp = c.enter_context(nc.psum_tensor("spp", [P, 2, 2, 512], F32))
            pvp = c.enter_context(nc.psum_tensor("pvp", [P, TB, 512], F32))
            space = Space(scratch)
            space.pools[0][1] = after_gates
            qs = space.cut(P, 2, NC, S)
            ks = space.cut(P, 2, NC, S)
            ew = space.cut(P, 2, 2, 2 * S)
            pw = space.cut(P, 2, 2, SW)
            pva = space.cut(P, NT, VA)
            sq = space.cut(P, NT, D)
            s_, a_, den, rec, ms, tt, rs, sc = (space.cut(P, NT * NH) for _ in range(8))
            NP2 = NH // 2
            SCALE = 1.0 / math.sqrt(DH)

            with nc.Block() as block:
                @block.sync
                def _(sp):
                    ctv = A["ctxT"].rearrange("(c p) t -> p c t", p=P)
                    with sp.Fori(0, B // 2) as k:
                        for u in range(2):
                            b = 2 * k + u
                            sp.wait_ge(s_ready, NP2 * b + NP2)
                            sp.dma_start(ks[:, u], ctv[:, :, bass.ds(b * S, S)]).then_inc(qk_in[u], 16)
                            sp.dma_start(qs[:, u], qT[:, :, bass.ds(b * S, S)]).then_inc(qk_in[u], 16)
                            load_w(sp, b + 1)
                    sp.wait_ge(qk_in[1], 32 * (B // 2))

                @block.tensor
                def _(pe):
                    pe.sem_inc(s_ready, 2 * NP2)
                    pe.sem_inc(pv_done, 2)

                    def decay_and_scores(b, u, p):
                        gidx = b * NP2 + p
                        pe.wait_ge(exp_done, gidx + 1)
                        for hh in range(2):
                            sel = pick[:, bass.ds(b * NH + 2 * p + hh, 1)].broadcast_to([P, P])
                            pe.matmul(wp[:, p % 2, hh, :], sel, parts, start=True, stop=False)
                            last = pe.matmul(wp[:, p % 2, hh, :], sel, parts2, start=False, stop=True)
                        last.then_inc(decay_ready, 1)
                        pe.wait_ge(mul_done, gidx + 1)
                        for hh in range(2):
                            hd = 2 * p + hh
                            rows, cc = slice(hd % 4 * DH, hd % 4 * DH + DH), hd // 4
                            pe.matmul(spp[:, p % 2, hh, 0:S], ks[rows, u, cc, 0:P], qs[rows, u, cc, :], start=True, stop=True)
                            last = pe.matmul(spp[:, p % 2, hh, S:SW], ks[rows, u, cc, P:S], qs[rows, u, cc, P:S], start=True, stop=True)
                        last.then_inc(s_ready, 1)

                    def values(b, p):
                        gidx = b * NP2 + p
                        pe.wait_ge(mul_done, gidx + 3)
                        if p == 0:
                            pe.wait_ge(pv_read, b + 1)
                        for hh in range(2):
                            hd = 2 * p + hh
                            cols = slice(hd * VH, hd * VH + VH)
                            v0, v1 = row(vaug, TB * b)[:, cols], row(vaug, TB * b + 1)[:, cols]
                            pe.matmul(pvp[:, 0, cols], pw[:, p % 2, hh, 0:P], v0, start=True, stop=True)
                            pe.matmul(pvp[:, 1, cols], pw[:, p % 2, hh, P:S], v0, start=True, stop=False)
                            last = pe.matmul(pvp[:, 1, cols], pw[:, p % 2, hh, S:SW], v1, start=False, stop=True)
                        last.then_inc(pv_done, 1)
                    with pe.Fori(0, B // 2) as k:
                        for u in range(2):
                            b = 2 * k + u
                            pe.wait_ge(qk_in[u], 32 * k + 32)
                            decay_and_scores(b, u, 0)
                            for p in range(1, NP2):
                                decay_and_scores(b, u, p)
                                values(b, p - 1)
                            values(b, NP2 - 1)

                @block.scalar
                def _(act):
                    act.sem_inc(exp_done, 2)
                    act.sem_inc(pv_read, 1)
                    with act.Fori(0, B // 2) as k:
                        for u in range(2):
                            b = 2 * k + u
                            for p in range(NP2):
                                gidx = b * NP2 + p
                                act.wait_ge(decay_ready, gidx + 1)
                                act.wait_ge(mul_done, gidx + 1)
                                for hh in range(2):
                                    n = b * NH + 2 * p + hh
                                    act.activation(ew[:, p % 2, hh, 0:S], wp[:, p % 2, hh, :], ACT.Exp, bias=bT[:, 0, bass.ds(n, 1)])
                                    last = act.activation(ew[:, p % 2, hh, S:SW], wp[:, p % 2, hh, P:S], ACT.Exp, bias=bT[:, 1, bass.ds(n, 1)])
                                last.then_inc(exp_done, 1)
                            act.wait_ge(pv_done, NP2 * b + NP2 + 2)
                            act.activation(row(pva, TB * b), pvp[:, 0, 0:VA], ACT.Copy)
                            act.activation(row(pva, TB * b + 1), pvp[:, 1, 0:VA], ACT.Copy).then_inc(pv_read, 1)
                    act.wait_ge(pv_read, B + 1)
                    act.activation(sq[:, :, :].rearrange("p k (h c) -> p (k h) c", c=DH),
                                   pva[:, :, :].rearrange("p k (h c) -> p (k h) c", c=VH)[:, :, 0:DH], ACT.Square).then_inc(sq_done, 1)

                @block.gpsimd
                def _(pool):
                    with pool.Fori(0, B // 2) as k:
                        for u in range(2):
                            b = 2 * k + u
                            for p in range(NP2):
                                gidx = b * NP2 + p
                                pool.wait_ge(exp_done, gidx + 3)
                                gate(pool)
                                diag = ew[:, p % 2].rearrange("p h (k c) -> p (h k) c", c=S)[:, :, 0:P]
                                pool.affine_select(out=diag, in_=diag, compare_op=ALU.is_ge, fill=0.0, base=0,
                                                   pattern=[[0, 4], [1, P]], channel_multiplier=-1).then_inc(masked, 1)
                                split_piece(pool, b, p, row(w1hi, b), row(w1lo, b))
                    pool.wait_ge(t_ready, 1)
                    pool.tensor_tensor(rs, tt, mhalf[:, :], ALU.pow).then_inc(r_ready, 1)
                    for i in range(4):
                        pool.wait_ge(y_ready, i + 1)
                        pool.tensor_tensor(sq[:, 4 * i:4 * i + 4, :], sq[:, 4 * i:4 * i + 4, :],
                                           gain.unsqueeze(1).broadcast_to([P, 4, D]), ALU.mult).then_inc(gained, 1)

                @block.vector
                def _(dve):
                    chain = Chain(dve, ch)
                    dve.sem_inc(mul_done, 2)
                    with dve.Fori(0, B // 2) as k:
                        for u in range(2):
                            b = 2 * k + u
                            for p in range(NP2):
                                gidx = b * NP2 + p
                                dve.wait_ge(masked, gidx + 1)
                                dve.wait_ge(s_ready, gidx + 1 + 2 * NP2)
                                dve.wait_ge(pv_done, gidx + 1)
                                dve.scalar_tensor_tensor(pw[:, p % 2], spp[:, p % 2, :, 0:SW], SCALE, ew[:, p % 2, :, 0:SW],
                                                         ALU.mult, ALU.mult).then_inc(mul_done, 1)
                    dve.wait_ge(pv_read, B + 1)
                    ph = pva[:, :, :].rearrange("p k (h c) -> p (k h) c", c=VH)
                    chain(dve.tensor_copy(s_, ph[:, :, DH:VH].rearrange("p n a -> p (n a)")))
                    chain(dve.scalar_tensor_tensor(a_, s_, -1.0, s_, ALU.mult, ALU.max))
                    chain(dve.tensor_tensor(den.rearrange("p (b t h) -> p b t h", b=B, t=TB), a_.rearrange("p (b t h) -> p b t h", b=B, t=TB),
                                            emT.rearrange("p t (b h) -> p b t h", b=B), ALU.max))
                    chain(dve.tensor_scalar(den, den, 5e-5, None, ALU.add))
                    chain(dve.reciprocal(rec, den))
                    dve.wait_ge(sq_done, 1)
                    chain(dve.tensor_reduce(ms, sq[:, :, :].rearrange("p k (h c) -> p (k h) c", c=DH), AX.X, ALU.add))
                    chain(dve.tensor_tensor(tt, rec, rec, ALU.mult))
                    chain(dve.tensor_tensor(tt, tt, ms, ALU.mult))
                    dve.tensor_scalar(tt, tt, 1.0 / DH, 1e-6, ALU.mult, ALU.add).then_inc(t_ready, 1)
                    dve.wait_ge(r_ready, 1)
                    chain(dve.tensor_tensor(sc, rs, rec, ALU.mult))
                    for i in range(4):
                        n = slice(4 * i * NH, (4 * i + 4) * NH)
                        dve.tensor_tensor(sq[:, 4 * i:4 * i + 4, :].rearrange("p k (h c) -> p (k h) c", c=DH), ph[:, n, 0:DH],
                                          wide(sc[:, n], DH), ALU.mult).then_inc(y_ready, 1)
                    for i in range(4):
                        dve.wait_ge(gained, i + 1)
                        last = dve.tensor_tensor(x_all[:, 4 * i:4 * i + 4, :], x_all[:, 4 * i:4 * i + 4, :], sq[:, 4 * i:4 * i + 4, :], ALU.add)
                    chain(last)

        space = Space(aux, region)
        w1q = space.cut(P, NC, F0, dt=BF16)
        w2q = space.cut(P, NF0, D, dt=BF16)
        b1bc = space.cut(P, F0)
        b2bc = space.cut(P, D)
        mw = space.cut(P, 2)
        with ExitStack() as c:
            sem = lambda n: c.enter_context(nc.semaphore("q_" + n))
            wq_in, b_in, ch, chp = sem("wq_in"), sem("b_in"), sem("dve_chain"), sem("pool_chain")
            var_ready, rstd_ready, r2_ready, v2_ready = sem("var_ready"), sem("rstd_ready"), sem("r2_ready"), sem("v2_ready")
            sum_ready, tot_ready, mw_ready = sem("sum_ready"), sem("tot_ready"), sem("mw_ready")
            tot = c.enter_context(nc.psum_tensor("tot", [P, 2], F32))
            raw_space = Space(scratch)
            raw1 = raw_space.cut(P, NC * F0)
            raw2 = raw_space.cut(P, NF0 * D)
            asum, rw, v2, r2 = raw_space.cut(P, 2), raw_space.cut(P, 2), raw_space.cut(P, NT), raw_space.cut(P, NT)

            def ternary(eng, chain, raw, scale, dst):
                chain(eng.tensor_scalar(raw, raw, scale, MAGIC, ALU.mult, ALU.add))
                chain(eng.tensor_scalar(raw, raw, MAGIC, 1.0, ALU.subtract, ALU.min))
                chain(eng.tensor_scalar(dst, raw, -1.0, None, ALU.max))

            with nc.Block() as block:
                @block.sync
                def _(sp):
                    sp.dma_start(raw1.rearrange("p (c f) -> p c f", c=NC), A["w1T"].rearrange("(c p) f -> p c f", p=P)).then_inc(wq_in, 16)
                    sp.dma_start(raw2.rearrange("p (c f) -> p c f", c=NF0), A["w2T"].rearrange("(c p) f -> p c f", p=P)).then_inc(wq_in, 16)
                    sp.dma_start(b1bc, A["b1"].partition_broadcast(P)).then_inc(b_in, 16)
                    sp.dma_start(b2bc, A["b2"].partition_broadcast(P)).then_inc(b_in, 16)
                    sp.wait_ge(b_in, 32)

                @block.tensor
                def _(pe):
                    pe.wait_ge(sum_ready, 1)
                    pe.matmul(tot[:, :], ones_f[:, :], asum, start=True, stop=True).then_inc(tot_ready, 1)

                @block.gpsimd
                def _(pool):
                    chain = Chain(pool, chp)
                    pool.wait_ge(var_ready, 1)
                    pool.tensor_tensor(rstd[:, :], veps[:, :], mhalf[:, 0:NT], ALU.pow).then_inc(rstd_ready, 1)
                    pool.wait_ge(v2_ready, 1)
                    pool.tensor_tensor(r2, v2, mhalf[:, 0:NT], ALU.pow).then_inc(r2_ready, 1)
                    pool.wait_ge(mw_ready, 1)
                    ternary(pool, chain, raw2, rw[:, 1:2], w2q.rearrange("p c f -> p (c f)"))

                @block.vector
                def _(dve):
                    chain = Chain(dve, ch)
                    layer_stats(dve, chain, var_ready)
                    dve.wait_ge(wq_in, 32)
                    dve.tensor_reduce(asum[:, 0:1], raw1, AX.X, ALU.add, apply_absolute_value=True)
                    dve.tensor_reduce(asum[:, 1:2], raw2, AX.X, ALU.add, apply_absolute_value=True).then_inc(sum_ready, 1)
                    dve.wait_ge(rstd_ready, 1)
                    chain(dve.tensor_tensor(v2, rstd[:, :], rstd[:, :], ALU.mult))
                    chain(dve.tensor_tensor(v2, v2, mv[:, :, 1], ALU.mult))
                    dve.tensor_scalar(v2, v2, 1e-5, None, ALU.add).then_inc(v2_ready, 1)
                    dve.wait_ge(tot_ready, 1)
                    chain(dve.tensor_scalar(mw, tot[:, :], 1.0 / (D * F0), 1e-5, ALU.mult, ALU.max))
                    dve.reciprocal(rw, mw).then_inc(mw_ready, 1)
                    dve.wait_ge(mw_ready, 1)
                    ternary(dve, chain, raw1, rw[:, 0:1], w1q.rearrange("p c f -> p (c f)"))
                    dve.wait_ge(r2_ready, 1)
                    chain(dve.tensor_tensor(rr[:, :], rstd[:, :], r2, ALU.mult))

        with ExitStack() as c:
            sem = lambda n: c.enter_context(nc.semaphore("f_" + n))
            ch, q_ready, tq_ready, qt_ready, h_ready = sem("dve_chain"), sem("q_ready"), sem("tq_ready"), sem("qt_ready"), sem("h_ready")
            hb_ready, g_ready, ssq_ready, ms_ready, r_ready = sem("hb_ready"), sem("g_ready"), sem("ssq_ready"), sem("ms_ready"), sem("r_ready")
            s2_ready, t_ready, q2_ready, t2_ready = sem("s2_ready"), sem("t_ready"), sem("q2_ready"), sem("t2_ready")
            q2t_ready, y_ready = sem("q2t_ready"), sem("y_ready")
            tqp = c.enter_context(nc.psum_tensor("tqp", [P, NC, P], BF16))
            hp = c.enter_context(nc.psum_tensor("hp", [P, F0], F32))
            t2p = c.enter_context(nc.psum_tensor("t2p", [P, NF0, P], BF16))
            yp = c.enter_context(nc.psum_tensor("yp", [P, D], F32))
            xb = space.cut(P, 2, D)
            qb = space.cut(P, 2, D, dt=BF16)
            qTb = space.cut(P, 2, NC, P, dt=BF16)
            hb = space.cut(P, 2, F0)

            q2b = space.cut(P, 2, F0, dt=BF16)
            q2T = space.cut(P, 2, NF0, P, dt=BF16)
            sm1 = space.cut(P, 2, 8)
            sm2 = space.cut(P, 2, 12)
            yt = space.cut(P, D)

            def run(eng, body, chain=None, k_steps=0):
                body(0, 0, True, False, False)
                body(1, 1, True, True, False)
                if chain:
                    chain.enter()
                with eng.Fori(0, (NT - 2) // 2) as k:
                    for u in range(2):
                        if chain:
                            chain.loop(2 * k + u, k_steps)
                        body(2 * k + 2 + u, u, True, True, True)
                        if chain:
                            chain.passed(k_steps)
                if chain:
                    chain.leave(NT - 2, k_steps)
                body(NT, 0, False, True, True)
                body(NT + 1, 1, False, False, True)

            with nc.Block() as block:
                @block.sync
                def _(sp):
                    with sp.Fori(0, E - 1) as k:
                        load_w(sp, k + E + 1)

                @block.gpsimd
                def _(pool):
                    def body(j, u, first, second, third):
                        if not second:
                            return
                        v, i = 1 - u, j - 1
                        pool.wait_ge(ms_ready, i + 1)
                        pool.tensor_tensor(sm2[:, v, 1:2], sm2[:, v, 0:1], mhalf[:, 0:1], ALU.pow).then_inc(r_ready, 1)
                        pool.wait_ge(s2_ready, i + 1)
                        gate(pool)
                        pool.tensor_scalar(hb[:, v], hb[:, v], sm2[:, v, 5:6], MAGIC, ALU.mult, ALU.add).then_inc(t_ready, 1)
                    body(0, 0, True, False, False)
                    body(1, 1, True, True, False)
                    with pool.Fori(0, (NT - 2) // 2) as k:
                        for u in range(2):
                            body(2 * k + 2 + u, u, True, True, True)
                            for q in range(2):
                                split_piece(pool, E + k, 2 * u + q, row(w2hi, k), row(w2lo, k))
                    body(NT, 0, False, True, True)
                    for q in range(SPLIT_PIECES):
                        split_piece(pool, 2 * E - 1, q, w2hi[:, E - 1], w2lo[:, E - 1])

                @block.tensor
                def _(pe):
                    def body(j, u, first, second, third):
                        if first:
                            pe.wait_ge(q_ready, j + 1)
                            for cc in range(NC):
                                last = pe.transpose(tqp[:, cc, :], qb[:, u, cc * P:(cc + 1) * P], identb[:, :])
                            last.then_inc(tq_ready, 1)
                            pe.wait_ge(qt_ready, j + 1)
                            if second:
                                pe.wait_ge(hb_ready, j)
                            for half in range(2):
                                for cc in range(NC):
                                    last = pe.matmul(hp[:, half * 512:(half + 1) * 512], qTb[:, u, cc, :],
                                                     w1q[:, cc, half * 512:(half + 1) * 512], start=(cc == 0), stop=(cc == NC - 1))
                            last.then_inc(h_ready, 1)
                        if second:
                            v = 1 - u
                            pe.wait_ge(q2_ready, j)
                            for f in range(NF0):
                                last = pe.transpose(t2p[:, f, :], q2b[:, v, f * P:(f + 1) * P], identb[:, :])
                            last.then_inc(t2_ready, 1)
                            pe.wait_ge(q2t_ready, j)
                            for f in range(NF0):
                                last = pe.matmul(yp[:, :], q2T[:, v, f, :], w2q[:, f, :], start=(f == 0), stop=(f == NF0 - 1))
                            last.then_inc(y_ready, 1)
                    run(pe, body)

                @block.scalar
                def _(act):
                    def body(j, u, first, second, third):
                        if first:
                            act.wait_ge(tq_ready, j + 1)
                            act.activation(qTb[:, u], tqp[:, :, :], ACT.Copy).then_inc(qt_ready, 1)
                            act.wait_ge(hb_ready, j + 1)
                            act.activation(hb[:, u], hb[:, u], ACT.Gelu).then_inc(g_ready, 1)
                            act.wait_ge(g_ready, j + 1)
                            act.activation(q2b[:, u], hb[:, u], ACT.Square, accum_out=sm2[:, u, 8:9]).then_inc(ssq_ready, 1)
                        if second:
                            act.wait_ge(t2_ready, j)
                            act.activation(q2T[:, 1 - u], t2p[:, :, :], ACT.Copy).then_inc(q2t_ready, 1)
                    run(act, body)

                @block.vector
                def _(dve):
                    chain = Chain(dve, ch)

                    def body(j, u, first, second, third):
                        v = 1 - u
                        if first:
                            w = sm1[:, u]
                            chain(dve.tensor_scalar(xb[:, u], tile_of(x_all, j),
                                                    col_of(mv, j), cell(rr[:, :], j), ALU.subtract, ALU.mult))
                            chain(dve.tensor_reduce(w[:, 0:1], xb[:, u], AX.X, ALU.max, apply_absolute_value=True))
                            chain(dve.tensor_scalar(w[:, 1:2], w[:, 0:1], 1e-5, None, ALU.max))
                            chain(dve.reciprocal(w[:, 2:3], w[:, 1:2]))
                            dve.tensor_scalar(w[:, 4:5], w[:, 1:2], 1.0 / 127.0, mw[:, 0:1], ALU.mult, ALU.mult)
                            chain(dve.tensor_scalar(w[:, 3:4], w[:, 2:3], 127.0, None, ALU.mult))
                            chain(dve.tensor_scalar(xb[:, u], xb[:, u], w[:, 3:4], MAGIC, ALU.mult, ALU.add))
                            dve.tensor_scalar(qb[:, u], xb[:, u], MAGIC, None, ALU.subtract).then_inc(q_ready, 1)
                        if second:
                            w = sm2[:, v]
                            dve.wait_ge(ssq_ready, j)
                            dve.tensor_scalar(w[:, 0:1], w[:, 8:9], 1.0 / F0, 1e-5, ALU.mult, ALU.add).then_inc(ms_ready, 1)
                            chain(dve.tensor_reduce(w[:, 2:3], hb[:, v], AX.X, ALU.max, apply_absolute_value=True))
                            dve.wait_ge(r_ready, j)
                            chain(dve.tensor_scalar(w[:, 3:4], w[:, 2:3], w[:, 1:2], 1e-5, ALU.mult, ALU.max))
                            chain(dve.reciprocal(w[:, 4:5], w[:, 3:4]))
                            dve.tensor_scalar(w[:, 6:7], w[:, 3:4], 1.0 / 127.0, mw[:, 1:2], ALU.mult, ALU.mult)
                            dve.tensor_scalar(w[:, 5:6], w[:, 4:5], 127.0, w[:, 1:2], ALU.mult, ALU.mult).then_inc(s2_ready, 1)
                        if third:
                            i = j - 2
                            xt = tile_of(x_all, i)
                            dve.wait_ge(y_ready, j - 1)
                            chain(dve.scalar_tensor_tensor(yt, yp[:, :], sm2[:, u, 6:7], b2bc, ALU.mult, ALU.add))
                            chain(dve.tensor_tensor(xt, xt, yt, ALU.add))
                        if first:
                            dve.wait_ge(h_ready, j + 1)
                            dve.scalar_tensor_tensor(hb[:, u], hp[:, :], sm1[:, u, 4:5], b1bc, ALU.mult, ALU.add).then_inc(hb_ready, 1)
                        if second:
                            dve.wait_ge(t_ready, j)
                            dve.tensor_scalar(q2b[:, v], hb[:, v], MAGIC, None, ALU.subtract).then_inc(q2_ready, 1)
                    run(dve, body, chain, 11)
        space = Space(aux, region)
        dmask = space.cut(P, SW)
        with ExitStack() as c:
            sem = lambda n: c.enter_context(nc.semaphore("n_" + n))
            ch, chp, var_ready, rstd_ready, dt_ready, ex_ready = (sem("dve_chain"), sem("pool_chain"), sem("var_ready"),
                                                                  sem("rstd_ready"), sem("dt_ready"), sem("ex_ready"))
            with nc.Block() as block:
                @block.gpsimd
                def _(pool):
                    chain = Chain(pool, chp)
                    pool.iota(dmask[:, 0:S], pattern=[[1, S]], base=0, channel_multiplier=-1, allow_small_or_imprecise_dtypes=True).then_inc(dt_ready, 1)
                    pool.wait_ge(var_ready, 1)
                    pool.tensor_tensor(rstd[:, :], veps[:, :], mhalf[:, 0:NT], ALU.pow).then_inc(rstd_ready, 1)
                    pool.wait_ge(ex_ready, 1)
                    chain(pool.affine_select(out=dmask[:, 0:P], in_=dmask[:, 0:P], compare_op=ALU.is_ge, fill=0.0, base=0,
                                             pattern=[[1, P]], channel_multiplier=-1))
                    chain(pool.tensor_copy(dmask[:, S:SW], dmask[:, 0:P]))

                @block.scalar
                def _(act):
                    act.wait_ge(dt_ready, 1)
                    act.activation(dmask[:, 0:S], dmask[:, 0:S], ACT.Exp, scale=LOG_FORGET).then_inc(ex_ready, 1)

                @block.vector
                def _(dve):
                    chain = Chain(dve, ch)
                    layer_stats(dve, chain, var_ready)

        with ExitStack() as c:
            sem = lambda n: c.enter_context(nc.semaphore("l_" + n))
            ch, xc_ready, tp_ready, e_ready, y_ready = sem("dve_chain"), sem("xc_ready"), sem("tp_ready"), sem("e_ready"), sem("y_ready")
            y4_ready, ph_ready, s_ready, w_ready, o_ready, sqs = (sem("y4_ready"), sem("ph_ready"), sem("s_ready"), sem("w_ready"),
                                                                  sem("o_ready"), sem("squares"))
            k_in = [sem("k_in0"), sem("k_in1")]
            tp = c.enter_context(nc.psum_tensor("ctp", [P, NC, S], F32))
            sps = c.enter_context(nc.psum_tensor("csp", [P, 512], F32))
            ops = c.enter_context(nc.psum_tensor("cop", [P, TB, 512], F32))
            xc = space.cut(P, TB, D)
            kst = space.cut(P, 2, NC * S)
            ex = space.cut(P, 2 * NC * S)
            up = space.cut(P, 2 * NC * S)
            y2 = space.cut(P, 2 * NC * S)
            ph = space.cut(P, 2, 2 * NC * S)
            wt = space.cut(P, 2, SW)
            den = space.cut(P, TB)
            H = NC * S

            def run(eng, body, chain=None, k_steps=0):
                body(0, 0, True, False)
                body(1, 1, True, True)
                if chain:
                    chain.enter()
                with eng.Fori(0, (B - 2) // 2) as k:
                    for u in range(2):
                        if chain:
                            chain.loop(2 * k + u, k_steps)
                        body(2 * k + 2 + u, u, True, True)
                        if chain:
                            chain.passed(k_steps)
                if chain:
                    chain.leave(B - 2, k_steps)
                body(B, 0, False, True)

            with nc.Block() as block:
                @block.sync
                def _(sp):
                    ctv = A["ctxT"].rearrange("(c p) t -> p c t", p=P)

                    def load(j, u):
                        sp.dma_start(kst[:, u].rearrange("p (c t) -> p c t", c=NC), ctv[:, :, bass.ds(j * S, S)]).then_inc(k_in[u], 16)
                    load(0, 0)
                    load(1, 1)
                    with sp.Fori(0, (B - 2) // 2) as k:
                        for u in range(2):
                            sp.wait_ge(y_ready, 2 * k + 1 + u)
                            load(2 * k + 2 + u, u)
                    sp.wait_ge(k_in[1], 16 * (B // 2))

                @block.vector
                def _(dve):
                    chain = Chain(dve, ch)

                    def body(j, u, first, second):
                        if first:
                            for t in range(TB):
                                i = TB * j + t
                                last = dve.tensor_scalar(xc[:, t], tile_of(x_all, i), col_of(mv, i), cell(rstd[:, :], i), ALU.subtract, ALU.mult)
                            last.then_inc(xc_ready, 1)
                        if second:
                            dve.wait_ge(s_ready, j)
                            dve.tensor_tensor(wt[:, 1 - u], sps[:, 0:SW], dmask, ALU.mult).then_inc(w_ready, 1)
                        if first:
                            if isinstance(j, int):
                                dve.wait_ge(k_in[u], 16 * (j // 2) + 16)
                            else:
                                dve.wait_ge(k_in[u], (j - u) * 8 + 16)
                            dve.tensor_scalar(up[:, H:2 * H], kst[:, u], 1.0, None, ALU.add)
                            dve.wait_ge(e_ready, j + 1)
                            chain(dve.tensor_scalar(up[:, 0:H], flat(tp[:, :, :]), 1.0, None, ALU.add))
                            dve.scalar_tensor_tensor(up, ex, 1.0, up, ALU.min, ALU.max).then_inc(y_ready, 1)
                        if second:
                            dve.wait_ge(o_ready, j)
                            chain(dve.tensor_scalar(den, ops[:, :, DH], 1e-8, None, ALU.add))
                            chain(dve.reciprocal(den, den))
                            for t in range(TB):
                                i = TB * (j - 1) + t
                                xt = tile_of(x_all, i).rearrange("p (h c) -> p h c", h=NH)
                                last = dve.scalar_tensor_tensor(xt, ops[:, t, 0:VA].rearrange("p (h c) -> p h c", h=NH)[:, :, 0:DH],
                                                                den[:, t:t + 1], xt, ALU.mult, ALU.add)
                            chain(last)
                    run(dve, body, chain, 4)

                @block.scalar
                def _(act):
                    def body(j, u, first, second):
                        if not first:
                            return
                        if isinstance(j, int):
                            act.wait_ge(k_in[u], 16 * (j // 2) + 16)
                        else:
                            act.wait_ge(k_in[u], (j - u) * 8 + 16)
                        if not isinstance(j, int) or j:
                            act.wait_ge(ph_ready, j)
                        act.activation(ex[:, H:2 * H], kst[:, u], ACT.Exp)
                        act.wait_ge(tp_ready, j + 1)
                        act.activation(ex[:, 0:H], flat(tp[:, :, :]), ACT.Exp).then_inc(e_ready, 1)
                        act.wait_ge(y_ready, j + 1)
                        act.activation(y2, up, ACT.Square).then_inc(sqs, 1)
                        act.wait_ge(sqs, j + 1)
                        act.activation(ex, y2, ACT.Square).then_inc(y4_ready, 1)
                    run(act, body)

                @block.gpsimd
                def _(pool):
                    def body(j, u, first, second):
                        if not first:
                            return
                        pool.wait_ge(y4_ready, j + 1)
                        pool.tensor_tensor(ph[:, u], ex, up, ALU.mult).then_inc(ph_ready, 1)
                    run(pool, body)

                @block.tensor
                def _(pe):
                    def body(j, u, first, second):
                        if first:
                            pe.wait_ge(xc_ready, j + 1)
                            if second:
                                pe.wait_ge(y_ready, j)
                            for t in range(TB):
                                for cc in range(NC):
                                    last = pe.transpose(tp[:, cc, t * P:(t + 1) * P], xc[:, t, cc * P:(cc + 1) * P], ident[:, :])
                            last.then_inc(tp_ready, 1)
                        if second:
                            v, b = 1 - u, j - 1
                            pe.wait_ge(ph_ready, j)
                            q = ph[:, v, 0:H].rearrange("p (c t) -> p c t", c=NC)
                            kk = ph[:, v, H:2 * H].rearrange("p (c t) -> p c t", c=NC)
                            for cc in range(NC):
                                pe.matmul(sps[:, 0:S], kk[:, cc, 0:P], q[:, cc, :], start=(cc == 0), stop=(cc == NC - 1))
                            for cc in range(NC):
                                last = pe.matmul(sps[:, S:SW], kk[:, cc, P:S], q[:, cc, P:S], start=(cc == 0), stop=(cc == NC - 1))
                            last.then_inc(s_ready, 1)
                            pe.wait_ge(w_ready, j)
                            v0, v1 = tile_of(vaug, TB * b), tile_of(vaug, TB * b + 1)
                            pe.matmul(ops[:, 0, 0:VA], wt[:, v, 0:P], v0, start=True, stop=True)
                            pe.matmul(ops[:, 1, 0:VA], wt[:, v, P:S], v0, start=True, stop=False)
                            pe.matmul(ops[:, 1, 0:VA], wt[:, v, S:SW], v1, start=False, stop=True).then_inc(o_ready, 1)
                    run(pe, body)

        packed = region.bitcast(BF16).rearrange("p (k n) -> p k n", k=NT)
        space = Space(aux, vaug_flat)
        slot = [space.cut(P, NT, dt=I32) for _ in range(2)]
        wgt = [space.cut(P, NT) for _ in range(2)]
        block_e = space.cut(P, NBLK, dt=I32)
        b1T = space.cut(P, E * NF)
        routing_at = [p[1] for p in space.pools]
        with ExitStack() as c:
            sem = lambda n: c.enter_context(nc.semaphore("r_" + n))
            ch, chp, var_ready, rstd_ready, small_in = sem("dve_chain"), sem("pool_chain"), sem("var_ready"), sem("rstd_ready"), sem("small_in")
            xn_ready, tp_ready, xt_ready, l_ready, hi_ready, lo_ready, lg_read = (sem("xn_ready"), sem("tp_ready"), sem("xt_ready"), sem("l_ready"),
                                                                         sem("hi_ready"), sem("lo_ready"), sem("lg_read"))
            tri_ready, c_ready, rank_ready, gap_ready, ex_ready, slot_ready, moved = (
                sem("tri_ready"), sem("c_ready"), sem("rank_ready"), sem("gap_ready"), sem("ex_ready"), sem("slot_ready"), sem("moved"))
            tp = c.enter_context(nc.psum_tensor("rtp", [P, NC, P], F32))
            lp = c.enter_context(nc.psum_tensor("rlp", [P, E], F32))
            rk = c.enter_context(nc.psum_tensor("rrk", [P, NT * E], F32))
            tot = c.enter_context(nc.psum_tensor("rtot", [P, E], F32))
            xs = space.cut(P, 2, D)
            xT = space.cut(P, 2, NC, P)
            wg = space.cut(P, NC, E)
            bg = space.cut(P, E)
            lg = space.cut(P, NT, E)
            NE = NT * E
            eq, pri, A1, A2, lg2, Cs, Ca, Cb, R, tmp = (space.cut(P, NT, E) for _ in range(10))
            low = space.cut(P, E)
            m1, m2, gap, e2, g1 = (space.cut(P, NT) for _ in range(5))
            Cbf = space.cut(P, NT, E, dt=BF16)
            Cex = space.cut(P, NT, E, dt=BF16)
            Cin = space.cut(P, E, dt=BF16)
            trib = space.cut(P, P, dt=BF16)
            oneb = space.cut(P, P, dt=BF16)
            cnt, nb, na, nb2, base = (space.cut(P, E) for _ in range(5))
            jj = space.cut(P, NBLK, E)
            jc = space.cut(P, NBLK, E)
            be = space.cut(P, NBLK)
            pos = space.cut(P, NT)
            with nc.Block() as block:
                @block.sync
                def _(sp):
                    sp.dma_start(wg, A["wg"].rearrange("(c p) e -> p c e", p=P)).then_inc(small_in, 16)
                    sp.dma_start(bg, A["bg"].partition_broadcast(P)).then_inc(small_in, 16)
                    sp.dma_start(b1T, A["eb1"]).then_inc(small_in, 16)
                    sp.wait_ge(small_in, 48)

                @block.gpsimd
                def _(pool):
                    chain = Chain(pool, chp)
                    pool.memset(oneb, 1.0)
                    chain(pool.memset(trib, 1.0))
                    pool.affine_select(out=trib, in_=trib, compare_op=ALU.is_gt, fill=0.0, base=0, pattern=[[1, P]],
                                       channel_multiplier=-1)
                    pool.iota(low, pattern=[[-1, E]], base=E, channel_multiplier=0, allow_small_or_imprecise_dtypes=True)
                    pool.iota(jj, pattern=[[1, NBLK], [0, E]], base=0, channel_multiplier=0, allow_small_or_imprecise_dtypes=True).then_inc(tri_ready, 1)
                    pool.wait_ge(var_ready, 1)
                    pool.tensor_tensor(rstd[:, :], veps[:, :], mhalf[:, 0:NT], ALU.pow).then_inc(rstd_ready, 1)
                    with pool.Fori(0, NT // 2) as k:
                        for u in range(2):
                            i = 2 * k + u
                            pool.wait_ge(hi_ready, i + 1)
                            pool.tensor_tensor(tile_of(packed, i)[:, D:2 * D], xs[:, u], tile_of(packed, i)[:, 0:D], ALU.subtract).then_inc(lo_ready, 1)
                    pool.wait_ge(lo_ready, NT + 1)
                    pool.wait_ge(slot_ready, 1)
                    pool.wait_ge(zero_in, 16 * NBLK * BT)
                    for i in range(NT):
                        for kx in range(2):
                            pool.indirect_dma_start(row_buf[:, :], bass.IndirectOffsetOnAxis(ap=slot[kx][:, i:i + 1], axis=0),
                                                    packed[:, i, :], None).then_inc(moved, 16)
                    pool.wait_ge(moved, 16 * 2 * NT)

                @block.scalar
                def _(act):
                    with act.Fori(0, NT // 2) as k:
                        for u in range(2):
                            i = 2 * k + u
                            act.wait_ge(xn_ready, i + 1)
                            act.activation(tile_of(packed, i)[:, 0:D], xs[:, u], ACT.Copy).then_inc(hi_ready, 1)
                            act.wait_ge(tp_ready, i + 1)
                            act.activation(xT[:, u], tp[:, :, :], ACT.Copy).then_inc(xt_ready, 1)
                    act.wait_ge(gap_ready, 1)
                    act.activation(e2, gap, ACT.Exp).then_inc(ex_ready, 1)

                @block.tensor
                def _(pe):
                    pe.sem_inc(xt_ready, 1)
                    pe.sem_inc(lg_read, 1)
                    pe.wait_ge(small_in, 48)
                    with pe.Fori(0, NT // 2) as k:
                        for u in range(2):
                            i = 2 * k + u
                            pe.wait_ge(xn_ready, i + 1)
                            pe.wait_ge(xt_ready, i + 1)
                            for cc in range(NC):
                                last = pe.transpose(tp[:, cc, :], xs[:, u, cc * P:(cc + 1) * P], ident[:, :])
                            last.then_inc(tp_ready, 1)
                            pe.wait_ge(xt_ready, i + 2)
                            pe.wait_ge(lg_read, i + 1)
                            for cc in range(NC):
                                last = pe.matmul(lp[:, :], xT[:, u, cc, :], wg[:, cc, :], start=(cc == 0), stop=(cc == NC - 1))
                            last.then_inc(l_ready, 1)
                    pe.wait_ge(tri_ready, 1)
                    pe.wait_ge(c_ready, 1)
                    pe.matmul(rk[:, :], trib, flat(Cbf), start=True, stop=False)
                    pe.matmul(rk[:, :], oneb, flat(Cex), start=False, stop=True)
                    pe.matmul(tot[:, :], oneb, Cin, start=True, stop=True).then_inc(rank_ready, 1)

                @block.vector
                def _(dve):
                    chain = Chain(dve, ch)
                    layer_stats(dve, chain, var_ready)
                    dve.sem_inc(lo_ready, 1)
                    dve.wait_ge(small_in, 48)
                    dve.wait_ge(rstd_ready, 1)
                    with dve.Fori(0, NT // 2) as k:
                        for u in range(2):
                            i = 2 * k + u
                            if u == 0:
                                dve.wait_ge(lo_ready, 2 * k + 1)
                            dve.tensor_scalar(xs[:, u], tile_of(x_all, i), col_of(mv, i), cell(rstd[:, :], i), ALU.subtract, ALU.mult).then_inc(xn_ready, 1)
                            dve.wait_ge(l_ready, i + 1)
                            dve.tensor_tensor(tile_of(lg, i), lp[:, :], bg, ALU.add).then_inc(lg_read, 1)
                    dve.wait_ge(lg_read, NT + 1)
                    dve.wait_ge(tri_ready, 1)

                    def choose(logits, top, onehot):
                        chain(dve.tensor_reduce(top, logits, AX.X, ALU.max))
                        chain(dve.tensor_tensor(eq, logits, wide(top, E), ALU.is_equal))
                        chain(dve.tensor_tensor(pri, eq, low.unsqueeze(1).broadcast_to([P, NT, E]), ALU.mult))
                        chain(dve.tensor_reduce(pos, pri, AX.X, ALU.max))
                        chain(dve.tensor_tensor(onehot, pri, wide(pos, E), ALU.is_equal))
                    choose(lg, m1, A1)
                    chain(dve.scalar_tensor_tensor(lg2, A1, LOWEST, lg, ALU.mult, ALU.add))
                    choose(lg2, m2, A2)
                    dve.tensor_tensor(gap, m2, m1, ALU.subtract).then_inc(gap_ready, 1)
                    chain(dve.tensor_tensor(Cs, A1, A2, ALU.add))
                    chain(dve.tensor_copy(Cbf, Cs))
                    src, dst = Cs, Ca
                    step = 1
                    while step < NT:
                        dve.tensor_copy(dst[:, 0:step], src[:, 0:step])
                        chain(dve.tensor_tensor(dst[:, step:], src[:, step:], src[:, :NT - step], ALU.add))
                        src, dst = dst, (Cb if dst is Ca else Ca)
                        step *= 2
                    chain(dve.tensor_copy(Cin, src[:, NT - 1]))
                    dve.tensor_tensor(Cex, src, Cs, ALU.subtract).then_inc(c_ready, 1)
                    dve.wait_ge(ex_ready, 1)
                    chain(dve.tensor_scalar(g1, e2, 1.0, None, ALU.add))
                    chain(dve.reciprocal(wgt[0], g1))
                    chain(dve.tensor_tensor(wgt[1], e2, wgt[0], ALU.mult))
                    dve.wait_ge(rank_ready, 1)
                    chain(dve.tensor_scalar(cnt, tot[:, :], float(BLK - 1), 1.0 / BLK, ALU.add, ALU.mult))
                    chain(dve.tensor_scalar(nb, cnt, 0.5 / BLK - 0.5, MAGIC, ALU.add, ALU.add))
                    chain(dve.tensor_scalar(nb, nb, MAGIC, None, ALU.subtract))
                    src, dst = nb, na
                    step = 1
                    while step < E:
                        dve.tensor_copy(dst[:, 0:step], src[:, 0:step])
                        chain(dve.tensor_tensor(dst[:, step:], src[:, step:], src[:, :E - step], ALU.add))
                        src, dst = dst, (nb2 if dst is na else na)
                        step *= 2
                    ends = src
                    chain(dve.tensor_tensor(base, ends, nb, ALU.subtract))
                    chain(dve.tensor_tensor(jc, jj, ends.unsqueeze(1).broadcast_to([P, NBLK, E]), ALU.is_ge))
                    chain(dve.tensor_reduce(be, jc, AX.X, ALU.add))
                    chain(dve.tensor_scalar(block_e, be, float(E - 1), None, ALU.min))
                    chain(dve.tensor_scalar(base, base, float(BLK), None, ALU.mult))
                    chain(dve.tensor_tensor(R, rk[:, :].rearrange("p (k e) -> p k e", k=NT), base.unsqueeze(1).broadcast_to([P, NT, E]), ALU.add))
                    for kx, onehot in ((0, A1), (1, A2)):
                        chain(dve.tensor_tensor(tmp, R, onehot, ALU.mult))
                        chain(dve.tensor_reduce(pos, tmp, AX.X, ALU.add))
                        chain(dve.tensor_copy(slot[kx], pos))
                    dve.sem_inc(slot_ready, 1)

        with ExitStack() as c:
            sem = lambda n: c.enter_context(nc.semaphore("e_" + n))
            tp_ready, xt_ready, gelu_done, hi_done, lo_done = sem("tp_ready"), sem("xt_ready"), sem("gelu_done"), sem("hi_done"), sem("lo_done")
            h_ready, m2_done, ys_ready, b_in = sem("h_ready"), sem("m2_done"), sem("ys_ready"), sem("b_in")
            x_in, y_out = [sem("x_in0"), sem("x_in1")], [sem("y_out0"), sem("y_out1")]
            space = Space(aux, vaug_flat, region, wstage[:, :])
            space.pools[0][1], space.pools[1][1] = routing_at[0], 0
            xg = space.cut(P, 2, BT * 2 * D, dt=BF16, pool=0)
            xT = space.cut(P, 2, 4, BLK, dt=BF16, pool=0)
            ys = space.cut(P, 2, BT * D, pool=0)
            hf = space.cut(P, 2, NF * BLK, pool=2)
            hhi = space.cut(P, 2, NF * BLK, dt=BF16, pool=1)
            hlo = space.cut(P, 2, NF * BLK, dt=BF16, pool=1)
            b2bc = space.cut(P, E * D, pool=3)
            tpp = c.enter_context(nc.psum_tensor("etp", [P, 4, BLK], BF16))
            hp = c.enter_context(nc.psum_tensor("ehp", [P, NF, BLK], F32))
            yp = c.enter_context(nc.psum_tensor("eyp", [P, 2, BT * D], F32))
            NQ, FQ = 4, NF // 4
            HB = FQ * BLK
            assert NBLK % 2 == 1

            with nc.Block() as block:
                @block.sync
                def _(sp):
                    sp.dma_start(b2bc, A["eb2"].partition_broadcast(P)).then_inc(b_in, 16)

                    def load(j, u):
                        sp.dma_start(xg[:, u].rearrange("p (t n) -> p t n", t=BT),
                                     row_buf[bass.ds(j * BLK, BLK), :].rearrange("(t p) n -> p t n", p=P)).then_inc(x_in[u], 16)

                    def store(i, v):
                        sp.wait_ge(ys_ready, i + 2)
                        sp.dma_start(y_buf[bass.ds(i * BLK, BLK), :].rearrange("(t p) n -> p t n", p=P),
                                     ys[:, v].rearrange("p (t n) -> p t n", t=BT)).then_inc(y_out[v], 16)
                    load(0, 0)
                    load(1, 1)
                    sp.wait_ge(tp_ready, 1)
                    load(2, 0)
                    with sp.Fori(0, (NBLK - 3) // 2) as k:
                        for u in range(2):
                            j = 2 * k + 1 + u
                            sp.wait_ge(tp_ready, j + 1)
                            load(j + 2, 1 - u)
                            store(j - 1, u)
                    for i in range(NBLK - 3, NBLK):
                        store(i, i % 2)
                    sp.wait_ge(y_out[0], 16 * ((NBLK + 1) // 2) + 16)
                    sp.wait_ge(y_out[1], 16 * (NBLK // 2) + 16)

                @block.tensor
                def _(pe):
                    pe.sem_inc(m2_done, 2)

                    def transposes(j, u, nth):
                        pe.wait_ge(x_in[u], 16 * nth + 16)
                        if not isinstance(j, int) or j:
                            pe.wait_ge(xt_ready, j)
                        for part in range(2):
                            for cc in range(NC):
                                for t in range(BT):
                                    c0 = t * 2 * D + part * D + cc * P
                                    last = pe.transpose(tpp[:, part * NC + cc, t * P:(t + 1) * P], xg[:, u, c0:c0 + P], identb[:, :])
                        last.then_inc(tp_ready, 1)

                    def matrix(w, e, at, n):
                        return w[:, bass.ds(e, 1), at:at + n].rearrange("p a n -> p (a n)")

                    def expert(j):
                        return pe.value_load(cell(block_e[0:1, :], j), min_val=0, max_val=E - 1)

                    def first_product(j, u, peeled=False):
                        e = expert(j)
                        pe.wait_ge(xt_ready, j + 1)
                        for f in range(NF):
                            if f % FQ == 0 and not peeled:
                                pe.wait_ge(gelu_done, (j - 1) * NQ + f // FQ + 1)
                            n = 0
                            for cc in range(NC):
                                hi_w, lo_w = matrix(w1hi, e, cc * FE + f * P, P), matrix(w1lo, e, cc * FE + f * P, P)
                                for w, part in ((hi_w, 0), (hi_w, 1), (lo_w, 0)):
                                    last = pe.matmul(hp[:, f, :], w, xT[:, u, part * NC + cc, :], start=(n == 0), stop=(n == 3 * NC - 1))
                                    n += 1
                            if f % FQ == FQ - 1:
                                last.then_inc(h_ready, 1)

                    def second_product(i, v):
                        e = expert(i)
                        pe.wait_ge(lo_done, NQ * i + 3 * NQ)
                        pe.wait_ge(ys_ready, i + 1)
                        for t in range(BT):
                            n = 0
                            for f in range(NF):
                                c0 = f * BLK + t * P
                                hi_w, lo_w = matrix(w2hi, e, f * D, D), matrix(w2lo, e, f * D, D)
                                for hpart, w in ((hhi, hi_w), (hhi, lo_w), (hlo, hi_w)):
                                    last = pe.matmul(yp[:, v, t * D:(t + 1) * D], hpart[:, v, c0:c0 + P], w, start=(n == 0), stop=(n == 3 * NF - 1))
                                    n += 1
                        last.then_inc(m2_done, 1)

                    transposes(0, 0, 0)
                    first_product(0, 0, peeled=True)
                    transposes(1, 1, 0)
                    with pe.Fori(0, (NBLK - 3) // 2) as k:
                        for u in range(2):
                            j = 2 * k + 1 + u
                            first_product(j, 1 - u)
                            transposes(j + 1, u, k + 1)
                            second_product(j - 1, u)
                    first_product(NBLK - 2, 1)
                    transposes(NBLK - 1, 0, (NBLK - 1) // 2)
                    second_product(NBLK - 3, 0)
                    first_product(NBLK - 1, 0)
                    second_product(NBLK - 2, 1)
                    second_product(NBLK - 1, 0)

                def passes(eng, fn):
                    with eng.Fori(0, (NBLK - 1) // 2) as k:
                        for u in range(2):
                            fn(2 * k + u, u)
                    fn(NBLK - 1, 0)

                @block.scalar
                def _(act):
                    def gelu(j, u):
                        e = act.value_load(cell(block_e[0:1, :], j), min_val=0, max_val=E - 1)
                        for q in range(NQ):
                            act.wait_ge(h_ready, NQ * j + q + 1)
                            act.wait_ge(lo_done, NQ * j + q + 1)
                            for f in range(FQ * q, FQ * q + FQ):
                                last = act.activation(hf[:, u, f * BLK:(f + 1) * BLK], hp[:, f, :], ACT.Gelu,
                                                      bias=b1T[:, bass.ds(e * NF + f, 1)])
                            last.then_inc(gelu_done, 1)
                    passes(act, gelu)

                @block.gpsimd
                def _(pool):
                    def high(j, u):
                        pool.wait_ge(m2_done, j + 1)
                        for q in range(NQ):
                            pool.wait_ge(gelu_done, NQ * j + q + 1)
                            gate(pool)
                            pool.tensor_copy(hhi[:, u, q * HB:(q + 1) * HB], hf[:, u, q * HB:(q + 1) * HB]).then_inc(hi_done, 1)
                    passes(pool, high)

                @block.vector
                def _(dve):
                    dve.sem_inc(ys_ready, 1)
                    dve.sem_inc(y_out[0], 16)
                    dve.sem_inc(y_out[1], 16)
                    dve.sem_inc(lo_done, 2 * NQ)
                    dve.wait_ge(b_in, 16)

                    def evacuate(j, u):
                        dve.wait_ge(tp_ready, j + 1)
                        dve.tensor_copy(xT[:, u], tpp[:, :, :]).then_inc(xt_ready, 1)

                    def low(j, u):
                        for q in range(NQ):
                            n = slice(q * HB, (q + 1) * HB)
                            dve.wait_ge(hi_done, NQ * j + q + 1)
                            dve.tensor_tensor(hlo[:, u, n], hf[:, u, n], hhi[:, u, n], ALU.subtract).then_inc(lo_done, 1)

                    def result(i, v, nth):
                        e = dve.value_load(cell(block_e[0:1, :], i), min_val=0, max_val=E - 1)
                        dve.wait_ge(m2_done, i + 3)
                        dve.wait_ge(y_out[v], 16 * nth + 16)
                        bias = b2bc.rearrange("p (e n) -> p e n", e=E)[:, bass.ds(e, 1)].broadcast_to([P, BT, D])
                        dve.tensor_tensor(ys[:, v].rearrange("p (t n) -> p t n", t=BT), yp[:, v].rearrange("p (t n) -> p t n", t=BT),
                                          bias, ALU.add).then_inc(ys_ready, 1)

                    evacuate(0, 0)
                    low(0, 0)
                    evacuate(1, 1)
                    with dve.Fori(0, (NBLK - 3) // 2) as k:
                        for u in range(2):
                            j = 2 * k + 1 + u
                            low(j, 1 - u)
                            evacuate(j + 1, u)
                            result(j - 1, u, k)
                    low(NBLK - 2, 1)
                    evacuate(NBLK - 1, 0)
                    result(NBLK - 3, 0, (NBLK - 3) // 2)
                    low(NBLK - 1, 0)
                    result(NBLK - 2, 1, (NBLK - 2) // 2)
                    result(NBLK - 1, 0, (NBLK - 1) // 2)

        with ExitStack() as c:
            NGR, GR = 4, NT // 4
            sem = lambda n: c.enter_context(nc.semaphore("o_" + n))
            got, done, stored, ch = [sem(f"gathered{k}") for k in range(NGR)], sem("done"), sem("stored"), sem("dve_chain")
            space = Space(region, vaug_flat)
            yg = [[space.cut(P, D) for _ in range(2)] for _ in range(NT)]
            with nc.Block() as block:
                @block.gpsimd
                def _(pool):
                    for i in range(NT):
                        for kx in range(2):
                            pool.indirect_dma_start(yg[i][kx], None, y_buf[:, :],
                                                    bass.IndirectOffsetOnAxis(ap=slot[kx][:, i:i + 1], axis=0)).then_inc(got[i // GR], 16)
                    for k in range(NGR):
                        pool.wait_ge(got[k], 16 * 2 * GR)

                @block.vector
                def _(dve):
                    chain = Chain(dve, ch)
                    for g in range(NGR):
                        dve.wait_ge(got[g], 16 * 2 * GR)
                        for kx in range(2):
                            for i in range(g * GR, g * GR + GR):
                                last = dve.scalar_tensor_tensor(x_all[:, i], yg[i][kx], wgt[kx][:, i:i + 1], x_all[:, i], ALU.mult, ALU.add)
                            if kx == 0:
                                chain(last)
                        last.then_inc(done, 1)

                @block.sync
                def _(sp):
                    xo = out.rearrange("(k p) d -> p k d", p=P)
                    for g in range(NGR):
                        sp.wait_ge(done, g + 1)
                        sp.dma_start(xo[:, g * GR:(g + 1) * GR, :], x_all[:, g * GR:(g + 1) * GR, :]).then_inc(stored, 16)
                    sp.wait_ge(stored, 16 * NGR)


_SHAPES = {"x": (T, D), "ctx": (T, D), "ctxT": (D, T), "ifwT": (3 * D, 2 * NH), "ifb": (P, 1), "outnorm": (D,),
           "w1T": (D, F0), "w2T": (F0, D), "b1": (F0,), "b2": (D,), "wg": (D, E), "bg": (E,),
           "wall": (2 * E, P, NC * FE), "eb1": (P, E * NF), "eb2": (E * D,)}


def kernel(x, ctx_1024, L0_xattn_ifgate_w, L0_xattn_ifgate_b, L0_xattn_outnorm_w, L0_ffn_w1, L0_ffn_b1, L0_ffn_w2, L0_ffn_b2,
           L1_ffn_Wg, L1_ffn_bg, L1_ffn_W1, L1_ffn_b1, L1_ffn_W2, L1_ffn_b2):
    import concourse.bacc as bacc
    from concourse.bass_utils import run_bass_kernel_spmd

    a = np.ascontiguousarray
    ctx = np.asarray(ctx_1024).reshape(T, D)
    ib = np.asarray(L0_xattn_ifgate_b)
    data = {
        "x": a(np.asarray(x).reshape(T, D)), "ctx": a(ctx), "ctxT": a(ctx.T),
        "ifwT": a(np.asarray(L0_xattn_ifgate_w).T),
        "ifb": a(np.concatenate([np.tile(ib[:NH], B), np.tile(ib[NH:], B)]).reshape(P, 1)),
        "outnorm": a(L0_xattn_outnorm_w),
        "w1T": a(np.asarray(L0_ffn_w1).T), "w2T": a(np.asarray(L0_ffn_w2).T), "b1": a(L0_ffn_b1), "b2": a(L0_ffn_b2),
        "wg": a(L1_ffn_Wg), "bg": a(L1_ffn_bg),
        "wall": a(np.concatenate([np.asarray(L1_ffn_W1).reshape(E, NC, P, FE).transpose(0, 2, 1, 3).reshape(E, P, NC * FE),
                                  np.asarray(L1_ffn_W2).reshape(E, NF, P, D).transpose(0, 2, 1, 3).reshape(E, P, NF * D)])),
        "eb1": a(np.asarray(L1_ffn_b1).reshape(E, NF, P).transpose(2, 0, 1).reshape(P, E * NF)),
        "eb2": a(np.asarray(L1_ffn_b2).reshape(E * D)),
    }
    nc = bacc.Bacc("TRN2", target_bir_lowering=False, num_devices=1)
    A = {n: nc.dram_tensor(f"in_{n}", s, F32, kind="ExternalInput").ap() for n, s in _SHAPES.items()}
    out = nc.dram_tensor("out_x", (T, D), F32, kind="ExternalOutput").ap()
    program(nc, A, out)
    r = run_bass_kernel_spmd(nc, [{f"in_{n}": v for n, v in data.items()}], core_ids=[0])
    return r.results[0]["out_x"].reshape(B, S, D)
```
